# Optimizing a Trainium2 kernel written in Bass

```python
import numpy as np
import jax
import jax.numpy as jnp

def _softmax(x, axis=-1):
    return jax.nn.softmax(x, axis=axis)

def _gelu(x):
    return jax.nn.gelu(x, approximate=True)

def _silu(x):
    return jax.nn.silu(x)

def _sigmoid(x):
    return jax.nn.sigmoid(x)

def _layernorm(x, axis=-1, eps=1e-05):
    m = jnp.mean(x, axis=axis, keepdims=True)
    v = jnp.var(x, axis=axis, keepdims=True)
    return (x - m) / jnp.sqrt(v + eps)

def _scatter_add(tgt, idx, src, axis=0):
    return tgt.at[idx].add(src)

def _segment_sum(src, seg, n):
    return jax.ops.segment_sum(src, seg, n)
kernel_name = 'mk_adj_resnorm_d2_adj_r2_572398'

def setup_inputs(seed: int=0):
    np.random.seed(seed)
    _w = jnp.asarray

    def _rec_inputs():
        import jax
        import jax.numpy as jnp
        _gk = jax.random.key(seed)
        x = -0.0002928 + 1 * jax.random.normal(jax.random.fold_in(_gk, 1), (4096, 256), jnp.float32)
        _a = jax.random.bernoulli(jax.random.fold_in(_gk, 2), 0.000488281, (4096, 4096))
        _a = jnp.logical_or(_a, jnp.eye(4096, dtype=bool))
        _af = _a.astype(jnp.float32)
        _af = _af * jax.random.uniform(jax.random.fold_in(_gk, 3), (4096, 4096), jnp.float32, 0.05, 1)
        adj = _af
        return (x, adj)
    x, adj = _rec_inputs()

    def _L0_gnn_setup():
        import jax, jax.numpy as jnp
        import numpy as np
        N = 4096
        IN_F = 256
        OUT_F = 256
        key = jax.random.key(seed)
        k1, k2, k3, k4 = jax.random.split(key, 4)
        input = jax.random.normal(k1, (N, IN_F), dtype=jnp.float32)
        adj = jax.random.uniform(k2, (N, N), dtype=jnp.float32)
        W = jax.random.normal(k3, (OUT_F, IN_F), dtype=jnp.float32) / np.sqrt(IN_F)
        b = jax.random.normal(k4, (OUT_F,), dtype=jnp.float32) * 0.01
        return {'input': input, 'adj': adj, 'W': W, 'b': b}
    _L0_gnn_all = _L0_gnn_setup()
    _L0_gnn_in = {k: v for k, v in _L0_gnn_all.items() if k in ('W', 'b')}
    del _L0_gnn_all

    def _L1_gnn_setup():
        import jax, jax.numpy as jnp
        import numpy as np
        EPS = 1e-08
        key = jax.random.key(seed)
        k1, k2, k3, k4 = jax.random.split(key, 4)
        N, IN, OUT = (4096, 256, 256)
        x = jax.random.normal(k1, (N, IN), dtype=jnp.float32)
        adj = jax.random.uniform(k2, (N, N), dtype=jnp.float32)
        W = jax.random.normal(k3, (OUT, IN), dtype=jnp.float32) * (1.0 / np.sqrt(IN))
        b = jax.random.normal(k4, (OUT,), dtype=jnp.float32) * 0.01
        return {'x': x, 'adj': adj, 'W': W, 'b': b}
    _L1_gnn_all = _L1_gnn_setup()
    _L1_gnn_in = {k: v for k, v in _L1_gnn_all.items() if k in ('W', 'b')}
    del _L1_gnn_all
    return {'x': x, 'adj': adj, 'L0_gnn_W': _L0_gnn_in['W'], 'L0_gnn_b': _L0_gnn_in['b'], 'L1_gnn_W': _L1_gnn_in['W'], 'L1_gnn_b': _L1_gnn_in['b']}

def reference(x, adj, L0_gnn_W, L0_gnn_b, L1_gnn_W, L1_gnn_b):
    import jax
    import jax.numpy as jnp

    def _L0_gnn_ref(input, adj, W, b):
        import jax, jax.numpy as jnp
        import numpy as np
        N = 4096
        IN_F = 256
        OUT_F = 256
        h = jnp.einsum('ni,oi->no', input, W) + b
        return adj @ h

    def _L1_gnn_ref(x, adj, W, b):
        import jax, jax.numpy as jnp
        import numpy as np
        EPS = 1e-08
        deg = adj.sum(axis=1)
        dis = (deg + EPS) ** (-0.5)
        a_norm = dis[:, None] * adj * dis[None, :]
        h = a_norm @ x
        return h @ W.T + b
    x = _layernorm(x + _L0_gnn_ref(x, adj, L0_gnn_W, L0_gnn_b), axis=-1)
    x = _layernorm(x + _L1_gnn_ref(x, adj, L1_gnn_W, L1_gnn_b), axis=-1)
    return x

_drawn_inputs = setup_inputs


def setup_inputs(seed=0):
    import zlib

    import numpy as np

    out = dict(_drawn_inputs(seed))
    spreads = {}
    factors = {'L0_gnn_b': 6.01, 'L1_gnn_b': 8.0}
    for name, (base, spread) in spreads.items():
        noise = np.random.default_rng([zlib.crc32(name.encode()), seed]).standard_normal(out[name].shape)
        drawn = base * np.exp(spread * noise) if base else spread * noise
        out[name] = jnp.asarray(drawn.astype(out[name].dtype))
    for name, factor in factors.items():
        out[name] = (out[name] * factor).astype(out[name].dtype)
    return out
```

```python
from contextlib import ExitStack

import concourse.bass as bass
from concourse import mybir

F32 = mybir.dt.float32
F32R = mybir.dt.float32r
ALU = mybir.AluOpType
ACT = mybir.ActivationFunctionType

P = 128
N = 4096
F = 256
LAYERS = 2
FH = F // P
WIDE = 512
ROWS = N // WIDE
IB = WIDE // P
JB = 4
CH = N // P // JB
RAW = 4
SPLIT = 2
LN_EPS = 1e-5
DEG_EPS = 1e-8
assert CH % RAW == 0 and CH % SPLIT == 0 and IB == JB


def same(g, n):
    return isinstance(g, int) and g == n


def graph_layers(nc, x, adj_t, w_t, biases, out):
    x_v = x.rearrange("(k j p) f -> k p j f", p=P, j=JB)
    out_v = out.rearrange("(r b p) f -> r p b f", p=P, b=IB)

    with ExitStack() as ctx:
        def sb(name, shape, dt=F32):
            return ctx.enter_context(nc.sbuf_tensor(name, shape, dt))

        def psum(name, shape):
            return ctx.enter_context(nc.psum_tensor(name, shape, F32))

        def sem(name):
            return ctx.enter_context(nc.semaphore(name))

        rows = sb("rows", [P, N // P, F])
        feat_hi = sb("feat_hi", [P, N // P, F], F32R)
        feat_lo = sb("feat_lo", [P, N // P, F], F32R)
        raw = sb("raw", [P, RAW, JB * WIDE])
        adj_hi = sb("adj_hi", [P, SPLIT, JB * WIDE], F32R)
        adj_lo = sb("adj_lo", [P, SPLIT, JB * WIDE], F32R)
        deg_acc = sb("deg_acc", [P, JB * WIDE])
        deg_part = sb("deg_part", [P, 2, WIDE])
        gath_hi = sb("gath_hi", [P, FH * WIDE], F32R)
        gath_lo = sb("gath_lo", [P, FH * WIDE], F32R)
        w_hi = sb("w_hi", [P, LAYERS, FH * F], F32R)
        w_lo = sb("w_lo", [P, LAYERS, FH * F], F32R)
        bias = sb("bias", [P, LAYERS, F])
        summed = sb("summed", [P, IB, F])
        done = sb("done", [P, IB, F])
        w_raw = done[:, :, :].rearrange("p (l h) o -> p l (h o)", l=LAYERS)
        ones = sb("ones", [P, 1])
        stats = sb("stats", [P, IB, 6])
        mean_var = sb("mean_var", [P, IB, 2])
        radicand = sb("radicand", [P, 2, IB])
        root = sb("root", [P, 2, IB])
        rstd = sb("rstd", [P, IB])
        dis = sb("dis", [P, N // P])

        gathered = psum("gathered", [P, 2, FH * WIDE])
        lin = psum("lin", [P, IB, F])
        deg = psum("deg", [P, IB])

        raw_loaded = [sem(f"raw_loaded{s}") for s in range(RAW)]
        x_loaded = [sem(f"x_loaded{k}") for k in range(CH)]
        w_loaded = sem("w_loaded")
        bias_loaded = sem("bias_loaded")
        out_stored = sem("out_stored")
        hi_ready = sem("hi_ready")
        lo_ready = sem("lo_ready")
        hi_used = sem("hi_used")
        chunk_used = sem("chunk_used")
        feat_hi_ready = sem("feat_hi_ready")
        feat_lo_ready = sem("feat_lo_ready")
        w_hi_ready = sem("w_hi_ready")
        w_lo_ready = sem("w_lo_ready")
        ones_ready = sem("ones_ready")
        deg_added = sem("deg_added")
        deg_folded = sem("deg_folded")
        deg_part_ready = sem("deg_part_ready")
        gath_hi_ready = sem("gath_hi_ready")
        gath_lo_ready = sem("gath_lo_ready")
        lin_ready = sem("lin_ready")
        lin_read = sem("lin_read")
        row_summed = sem("row_summed")
        row_stats = sem("row_stats")
        row_moments = sem("row_moments")
        radicand_ready = sem("radicand_ready")
        root_ready = sem("root_ready")
        rstd_ready = sem("rstd_ready")
        rows_done = sem("rows_done")

        def half(t, s, h, n):
            return t[:, s, h * n:(h + 1) * n]

        with nc.Block() as block:

            @block.sync
            def _(sp):
                def load_chunk(g, row, k):
                    sp.dma_start(raw[:, k % RAW, :].rearrange("p (j i) -> p j i", j=JB),
                                 adj_t[row, k]).then_inc(raw_loaded[k % RAW], 16)

                def load_row_layer0(g):
                    for k in range(CH):
                        before = k - RAW
                        if before >= 1:
                            sp.wait_ge(deg_added, (CH - 1) * g + before)
                        elif before == 0:
                            sp.wait_ge(deg_added, (CH - 1) * g + 1)
                        else:
                            sp.wait_ge(deg_added, (CH - 1) * (g - 1) + before + CH)
                        load_chunk(g, g, k)

                def load_row_layer1(g, store):
                    for k in range(CH):
                        sp.wait_ge(lo_ready, CH * g + k - RAW + 1)
                        load_chunk(g, g - ROWS, k)
                        if store and k == 1:
                            store_row(g - 2)

                def store_row(g):
                    sp.wait_ge(rows_done, g + 1)
                    sp.dma_start(out_v[g - ROWS], done[:, :, :]).then_inc(out_stored, 16)

                for k in range(CH):
                    sp.dma_start(rows[:, k * JB:(k + 1) * JB, :], x_v[k]).then_inc(x_loaded[k], 16)
                    if k >= RAW:
                        sp.wait_ge(deg_added, max(k - RAW, 1))
                    load_chunk(0, 0, k)
                    if k == 0:
                        sp.dma_start(w_raw, w_t.rearrange("l p h o -> p l (h o)")).then_inc(w_loaded, 16)
                        sp.dma_start(bias[:, :, :], biases.partition_broadcast(P)).then_inc(bias_loaded, 16)
                with sp.Fori(1, ROWS) as g:
                    load_row_layer0(g)
                for k in range(CH):
                    if k < RAW:
                        sp.wait_ge(deg_added, (CH - 1) * (ROWS - 1) + k - RAW + CH)
                    else:
                        sp.wait_ge(lo_ready, CH * ROWS + k - RAW + 1)
                    load_chunk(ROWS, 0, k)
                load_row_layer1(ROWS + 1, store=False)
                with sp.Fori(ROWS + 2, 2 * ROWS) as g:
                    load_row_layer1(g, store=True)
                for g in (2 * ROWS - 2, 2 * ROWS - 1):
                    store_row(g)
                sp.wait_ge(out_stored, 16 * ROWS)

            @block.scalar
            def _(act):
                def split_chunk(g, k):
                    act.wait_ge(raw_loaded[k % RAW], 16 * (CH // RAW * g + k // RAW + 1))
                    if not (isinstance(g, int) and CH * g + k < SPLIT):
                        act.wait_ge(hi_used, CH * g + k - SPLIT + 1)
                        act.wait_ge(lo_ready, CH * g + k - SPLIT + 1)
                    nc.scalar.copy(adj_hi[:, k % SPLIT, :], raw[:, k % RAW, :]).then_inc(hi_ready, 1)

                def split_gathered(g):
                    act.wait_ge(chunk_used, CH * (g + 1))
                    if not (same(g, 0)):
                        act.wait_ge(lin_ready, IB * g)
                    nc.scalar.copy(gath_hi[:, :], gathered[:, g % 2, :]).then_inc(gath_hi_ready, 1)

                def roots(g, layer):
                    n = 2 if layer == 0 else 1
                    act.wait_ge(radicand_ready, g + 1)
                    nc.scalar.activation(root[:, 0:n, :], radicand[:, 0:n, :], ACT.Sqrt).then_inc(root_ready, 1)

                def row(g, layer):
                    for k in range(CH):
                        if k == 1:
                            split_gathered(g - 1)
                        split_chunk(g, k)
                        if k == 5:
                            roots(g - 1, layer)

                for k in range(CH):
                    act.wait_ge(x_loaded[k], 16)
                    blocks = slice(k * JB, (k + 1) * JB)
                    nc.scalar.copy(feat_hi[:, blocks, :], rows[:, blocks, :]).then_inc(feat_hi_ready, 1)
                    split_chunk(0, k)
                    if k == 1:
                        act.wait_ge(w_loaded, 16)
                        nc.scalar.copy(w_hi[:, :, :], w_raw).then_inc(w_hi_ready, 1)
                row(1, 0)
                with act.Fori(2, ROWS) as g:
                    row(g, 0)
                for k in range(CH):
                    if k == 1:
                        split_gathered(ROWS - 1)
                    act.wait_ge(rows_done, k + 1)
                    act.wait_ge(chunk_used, CH * (ROWS - 1) + k + 1)
                    for j in range(k * JB, (k + 1) * JB):
                        last = nc.scalar.activation(feat_hi[:, j, :], rows[:, j, :], ACT.Copy,
                                                    scale=dis[:, j:j + 1])
                    last.then_inc(feat_hi_ready, 1)
                    split_chunk(ROWS, k)
                    if k == 5:
                        roots(ROWS - 1, 0)
                with act.Fori(ROWS + 1, 2 * ROWS) as g:
                    row(g, 1)
                split_gathered(2 * ROWS - 1)
                roots(2 * ROWS - 1, 1)

            @block.vector
            def _(dve):
                def split_chunk(g, k):
                    dve.wait_ge(hi_ready, CH * g + k + 1)
                    if not (isinstance(g, int) and CH * g + k < SPLIT):
                        dve.wait_ge(chunk_used, CH * g + k - SPLIT + 1)
                    nc.vector.tensor_tensor(adj_lo[:, k % SPLIT, :], raw[:, k % RAW, :],
                                            adj_hi[:, k % SPLIT, :].bitcast(F32),
                                            ALU.subtract).then_inc(lo_ready, 1)

                def add_degrees(g, k):
                    if k == 1:
                        if not (same(g, 0)):
                            dve.wait_ge(deg_part_ready, g)
                        nc.vector.tensor_tensor(deg_acc[:, :], raw[:, 0, :], raw[:, 1, :],
                                                ALU.add).then_inc(deg_added, 1)
                    elif k > 1:
                        dve.wait_ge(deg_added, (CH - 1) * g + k - 1)
                        nc.vector.tensor_tensor(deg_acc[:, :], deg_acc[:, :], raw[:, k % RAW, :],
                                                ALU.add).then_inc(deg_added, 1)
                    if k == CH - 1:
                        dve.wait_ge(deg_added, (CH - 1) * (g + 1))
                        nc.vector.tensor_tensor(deg_acc[:, 0:2 * WIDE], deg_acc[:, 0:2 * WIDE],
                                                deg_acc[:, 2 * WIDE:4 * WIDE], ALU.add).then_inc(deg_folded, 1)
                        dve.wait_ge(deg_folded, g + 1)
                        nc.vector.tensor_tensor(deg_part[:, g % 2, :], deg_acc[:, 0:WIDE],
                                                deg_acc[:, WIDE:2 * WIDE], ALU.add).then_inc(deg_part_ready, 1)

                def split_gathered(g):
                    dve.wait_ge(gath_hi_ready, g + 1)
                    nc.vector.tensor_tensor(gath_lo[:, :], gathered[:, g % 2, :], gath_hi[:, :].bitcast(F32),
                                            ALU.subtract).then_inc(gath_lo_ready, 1)

                def sum_rows(g, row, layer):
                    if not (same(g, 0)):
                        dve.wait_ge(rows_done, g)
                    for b in range(IB):
                        dve.wait_ge(lin_ready, IB * g + b + 2 - b % 2)
                        if layer == 0:
                            nc.vector.scalar_tensor_tensor(
                                summed[:, b, :], bias[:, 0, :], deg[:, b:b + 1], lin[:, b, :],
                                ALU.mult, ALU.add).then_inc(lin_read, 1)
                        else:
                            nc.vector.scalar_tensor_tensor(
                                summed[:, b, :], lin[:, b, :], dis[:, bass.ds(row * IB + b, 1)],
                                rows[:, row * IB + b, :], ALU.mult, ALU.add).then_inc(lin_read, 1)
                    for b in range(IB):
                        dve.wait_ge(lin_read, IB * g + b + 1)
                        other = rows[:, row * IB + b, :] if layer == 0 else bias[:, 1, :]
                        nc.vector.tensor_tensor(summed[:, b, :], summed[:, b, :], other,
                                                ALU.add).then_inc(row_summed, 1)
                    for b in range(IB):
                        dve.wait_ge(row_summed, IB * g + b + 1)
                        nc.vector.bn_stats(stats[:, b, :], summed[:, b, :]).then_inc(row_stats, 1)

                def stats_written(g):
                    dve.wait_ge(row_stats, IB * (g + 1))

                def moments(g, layer):
                    for b in range(IB):
                        nc.vector.bn_aggr(mean_var[:, b, :], stats[:, b, :]).then_inc(row_moments, 1)
                    if layer == 0:
                        nc.vector.tensor_scalar_add(radicand[:, 1, :], deg[:, :], DEG_EPS)
                    dve.wait_ge(row_moments, IB * (g + 1))
                    nc.vector.tensor_scalar_add(radicand[:, 0, :], mean_var[:, :, 1],
                                                LN_EPS).then_inc(radicand_ready, 1)

                def normalise(g, row, layer):
                    dve.wait_ge(root_ready, g + 1)
                    if layer == 0:
                        nc.vector.reciprocal(dis[:, bass.ds(row * IB, IB)], root[:, 1, :])
                    nc.vector.reciprocal(rstd[:, :], root[:, 0, :]).then_inc(rstd_ready, 1)
                    dve.wait_ge(rstd_ready, g + 1)
                    if layer == 1 and not (same(g, ROWS)):
                        dve.wait_ge(out_stored, 16 * (g - ROWS))
                    for b in range(IB):
                        into = rows[:, row * IB + b, :] if layer == 0 else done[:, b, :]
                        last = nc.vector.tensor_scalar(into, summed[:, b, :], mean_var[:, b, 0:1],
                                                       rstd[:, b:b + 1], ALU.subtract, ALU.mult)
                    last.then_inc(rows_done, 1)

                def end_step(g, row, layer, k):
                    if k == 0:
                        split_gathered(g)
                    if k == 2:
                        sum_rows(g, row, layer)
                    if k == 3:
                        moments(g, layer)
                    if k == 5:
                        normalise(g, row, layer)

                def row(g, layer):
                    for k in range(CH):
                        if k == 3:
                            stats_written(g - 1)
                        split_chunk(g, k)
                        if layer == 0:
                            add_degrees(g, k)
                        end_step(g - 1, g - 1 - layer * ROWS, layer, k)

                nc.vector.memset(ones[:, :], 1.0).then_inc(ones_ready, 1)
                for k in range(CH):
                    blocks = slice(k * JB, (k + 1) * JB)
                    dve.wait_ge(feat_hi_ready, k + 1)
                    nc.vector.tensor_tensor(feat_lo[:, blocks, :], rows[:, blocks, :],
                                            feat_hi[:, blocks, :].bitcast(F32),
                                            ALU.subtract).then_inc(feat_lo_ready, 1)
                    split_chunk(0, k)
                    add_degrees(0, k)
                    if k == 1:
                        dve.wait_ge(w_hi_ready, 1)
                        nc.vector.tensor_tensor(w_lo[:, :, :], w_raw, w_hi[:, :, :].bitcast(F32),
                                                ALU.subtract).then_inc(w_lo_ready, 1)
                dve.wait_ge(bias_loaded, 16)
                row(1, 0)
                with dve.Fori(2, ROWS) as g:
                    row(g, 0)
                for k in range(CH):
                    dve.wait_ge(feat_hi_ready, CH + k + 1)
                    for j in range(k * JB, (k + 1) * JB):
                        last = nc.vector.scalar_tensor_tensor(
                            feat_lo[:, j, :], rows[:, j, :], dis[:, j:j + 1], feat_hi[:, j, :].bitcast(F32),
                            ALU.mult, ALU.subtract)
                    last.then_inc(feat_lo_ready, 1)
                    if k == 3:
                        stats_written(ROWS - 1)
                    split_chunk(ROWS, k)
                    end_step(ROWS - 1, ROWS - 1, 0, k)
                row(ROWS + 1, 1)
                with dve.Fori(ROWS + 2, 2 * ROWS) as g:
                    row(g, 1)
                for k in range(CH):
                    if k == 3:
                        stats_written(2 * ROWS - 1)
                    end_step(2 * ROWS - 1, ROWS - 1, 1, k)

            @block.tensor
            def _(pe):
                def chunk(g, parity, k):
                    pe.wait_ge(hi_ready, CH * g + k + 1)
                    if isinstance(g, int) and g % ROWS == 0:
                        pe.wait_ge(feat_hi_ready, CH * (g // ROWS) + k + 1)
                        pe.wait_ge(feat_lo_ready, CH * (g // ROWS) + k + 1)
                    for j in range(JB):
                        for h in range(FH):
                            for feat in (feat_hi, feat_lo):
                                last = nc.tensor.matmul(
                                    half(gathered, parity, h, WIDE), half(feat, k * JB + j, h, P),
                                    half(adj_hi, k % SPLIT, j, WIDE),
                                    start=(k == 0 and j == 0 and feat is feat_hi), stop=False)
                    last.then_inc(hi_used, 1)
                    pe.wait_ge(lo_ready, CH * g + k + 1)
                    for j in range(JB):
                        for h in range(FH):
                            last = nc.tensor.matmul(
                                half(gathered, parity, h, WIDE), half(feat_hi, k * JB + j, h, P),
                                half(adj_lo, k % SPLIT, j, WIDE),
                                start=False, stop=(k == CH - 1 and j == JB - 1))
                    last.then_inc(chunk_used, 1)

                def linear(g, parity, layer):
                    if not (same(g, 0)):
                        pe.wait_ge(lin_read, IB * g)
                    if layer == 0:
                        if same(g, 0):
                            pe.wait_ge(ones_ready, 1)
                            pe.wait_ge(w_lo_ready, 1)
                        else:
                            pe.wait_ge(radicand_ready, g)
                        pe.wait_ge(deg_part_ready, g + 1)
                        for b in range(IB):
                            nc.tensor.matmul(deg[:, b:b + 1], half(deg_part, parity, b, P), ones[:, :],
                                             start=True, stop=True)
                    pe.wait_ge(gath_hi_ready, g + 1)
                    pe.wait_ge(gath_lo_ready, g + 1)
                    for b in range(IB):
                        for h in range(FH):
                            columns = slice(h * WIDE + b * P, h * WIDE + (b + 1) * P)
                            for gath, w in ((gath_hi, w_hi), (gath_hi, w_lo), (gath_lo, w_hi)):
                                last = nc.tensor.matmul(
                                    lin[:, b, :], gath[:, columns], half(w, layer, h, F),
                                    start=(h == 0 and gath is gath_hi and w is w_hi),
                                    stop=(h == FH - 1 and gath is gath_lo))
                        last.then_inc(lin_ready, 1)

                def row(g, parity, layer):
                    chunk(g, parity, 0)
                    linear(g - 1, 1 - parity, layer)
                    for k in range(1, CH):
                        chunk(g, parity, k)

                for k in range(CH):
                    chunk(0, 0, k)
                row(1, 1, 0)
                with pe.Fori(2, ROWS, 2) as g:
                    row(g, 0, 0)
                    row(g + 1, 1, 0)
                row(ROWS, 0, 0)
                with pe.Fori(ROWS + 1, 2 * ROWS - 1, 2) as g:
                    row(g, 1, 1)
                    row(g + 1, 0, 1)
                row(2 * ROWS - 1, 1, 1)
                linear(2 * ROWS - 1, 1, 1)


def kernel(x, adj, L0_gnn_W, L0_gnn_b, L1_gnn_W, L1_gnn_b):
    import numpy as np
    import concourse.bacc as bacc
    from concourse.bass_utils import run_bass_kernel_spmd

    adj_t = np.ascontiguousarray(
        np.asarray(adj).reshape(ROWS, WIDE, CH, JB, P).transpose(0, 2, 4, 3, 1))
    w_t = np.ascontiguousarray(np.stack(
        [np.asarray(w).T.reshape(FH, P, F).transpose(1, 0, 2) for w in (L0_gnn_W, L1_gnn_W)]))
    arrays = {
        "x": np.ascontiguousarray(x), "adj_t": adj_t, "w_t": w_t,
        "biases": np.stack([np.asarray(L0_gnn_b), np.asarray(L1_gnn_b)]),
    }
    nc = bacc.Bacc("TRN2", target_bir_lowering=False, num_devices=1)
    args = [nc.dram_tensor(n, a.shape, mybir.dt.from_np(a.dtype), kind="ExternalInput").ap()
            for n, a in arrays.items()]
    out = nc.dram_tensor("out", (N, F), F32, kind="ExternalOutput").ap()
    graph_layers(nc, *args, out)
    got = run_bass_kernel_spmd(nc, [arrays], core_ids=[0])
    return got.results[0]["out"]
```

```python
from contextlib import ExitStack

import concourse.bass as bass
from concourse import mybir

F32 = mybir.dt.float32
F32R = mybir.dt.float32r
ALU = mybir.AluOpType
ACT = mybir.ActivationFunctionType

P = 128
N = 4096
F = 256
LAYERS = 2
FH = F // P
WIDE = 512
ROWS = N // WIDE
IB = WIDE // P
JB = 4
CH = N // P // JB
RAW = 4
SPLIT = 2
LN_EPS = 1e-5
DEG_EPS = 1e-8
EARLY = 2
assert EARLY == SPLIT and CH % RAW == 0 and CH % SPLIT == 0 and IB == JB


def same(g, n):
    return isinstance(g, int) and g == n


def graph_layers(nc, x, adj_t, w_t, biases, out):
    x_v = x.rearrange("(k j p) f -> k p j f", p=P, j=JB)
    out_v = out.rearrange("(r b p) f -> r p b f", p=P, b=IB)

    with ExitStack() as ctx:
        def sb(name, shape, dt=F32):
            return ctx.enter_context(nc.sbuf_tensor(name, shape, dt))

        def psum(name, shape):
            return ctx.enter_context(nc.psum_tensor(name, shape, F32))

        def sem(name):
            return ctx.enter_context(nc.semaphore(name))

        rows = sb("rows", [P, N // P, F])
        feat_hi = sb("feat_hi", [P, N // P, F], F32R)
        feat_lo = sb("feat_lo", [P, N // P, F], F32R)
        raw = sb("raw", [P, RAW, JB * WIDE])
        adj_hi = sb("adj_hi", [P, SPLIT, JB * WIDE], F32R)
        adj_lo = sb("adj_lo", [P, SPLIT, JB * WIDE], F32R)
        deg_acc = sb("deg_acc", [P, JB * WIDE])
        deg_part = sb("deg_part", [P, WIDE])
        gath_hi = sb("gath_hi", [P, FH * WIDE], F32R)
        gath_lo = sb("gath_lo", [P, FH * WIDE], F32R)
        w_hi = sb("w_hi", [P, LAYERS, FH * F], F32R)
        w_lo = sb("w_lo", [P, LAYERS, FH * F], F32R)
        bias = sb("bias", [P, LAYERS, F])
        summed = sb("summed", [P, IB, F])
        done = sb("done", [P, IB, F])
        w_raw = done[:, :, :].rearrange("p (l h) o -> p l (h o)", l=LAYERS)
        ones = sb("ones", [P, 1])
        eps = sb("eps", [P, 2])
        stats = sb("stats", [P, IB, 6])
        mean_var = sb("mean_var", [P, IB, 2])
        root = sb("root", [P, 2, IB])
        rstd = sb("rstd", [P, IB])
        shift = sb("shift", [P, IB])
        dis = sb("dis", [P, N // P])

        gathered = psum("gathered", [P, 2, FH * WIDE])
        lin = psum("lin", [P, IB, F])
        deg = psum("deg", [P, IB])

        raw_loaded = [sem(f"raw_loaded{s}") for s in range(RAW)]
        x_loaded = [sem(f"x_loaded{k}") for k in range(EARLY, CH)]
        piece_loaded = [sem(f"piece_loaded{q}") for q in range(EARLY * JB)]
        w_loaded = sem("w_loaded")
        bias_loaded = sem("bias_loaded")
        out_stored = sem("out_stored")
        hi_ready = sem("hi_ready")
        lo_ready = sem("lo_ready")
        hi_used = sem("hi_used")
        chunk_used = sem("chunk_used")
        feat_hi_ready = sem("feat_hi_ready")
        feat_lo_ready = sem("feat_lo_ready")
        piece_hi_ready = sem("piece_hi_ready")
        piece_feat_lo_ready = sem("piece_feat_lo_ready")
        piece_lo_ready = sem("piece_lo_ready")
        w_hi_ready = sem("w_hi_ready")
        w_lo_ready = sem("w_lo_ready")
        constants_ready = sem("constants_ready")
        deg_added = sem("deg_added")
        deg_folded = sem("deg_folded")
        deg_part_ready = sem("deg_part_ready")
        deg_ready = sem("deg_ready")
        gath_hi_ready = sem("gath_hi_ready")
        gath_lo_ready = sem("gath_lo_ready")
        lin_ready = sem("lin_ready")
        lin_read = sem("lin_read")
        row_summed = sem("row_summed")
        row_stats = sem("row_stats")
        row_moments = sem("row_moments")
        root_ready = sem("root_ready")
        rstd_ready = sem("rstd_ready")
        shift_ready = sem("shift_ready")
        rows_done = sem("rows_done")
        half_summed = sem("half_summed")
        half_hi_ready = sem("half_hi_ready")
        residual_ready = sem("residual_ready")
        block_done = sem("block_done")

        last_lin = [lin[:, 0, :], lin[:, 2, :], gathered[:, 0, 0:F], gathered[:, 0, WIDE:WIDE + F]]

        def half(t, s, h, n):
            return t[:, s, h * n:(h + 1) * n]

        def piece_ready(engine, of_pieces, of_chunks, q):
            if q % JB < JB - 1:
                engine.wait_ge(of_pieces, q - q // JB + 1)
            else:
                engine.wait_ge(of_chunks, q // JB + 1)

        with nc.Block() as block:

            @block.sync
            def _(sp):
                def load_chunk(g, row, k):
                    sp.dma_start(raw[:, k % RAW, :].rearrange("p (j i) -> p j i", j=JB),
                                 adj_t[row, k]).then_inc(raw_loaded[k % RAW], 16)

                def load_row_layer0(g):
                    for k in range(CH):
                        before = k - RAW
                        if before >= 1:
                            sp.wait_ge(deg_added, (CH - 1) * g + before)
                        elif before == 0:
                            sp.wait_ge(deg_added, (CH - 1) * g + 1)
                        else:
                            sp.wait_ge(deg_added, (CH - 1) * (g - 1) + before + CH)
                        load_chunk(g, g, k)

                def load_row_layer1(g, store):
                    for k in range(CH):
                        sp.wait_ge(lo_ready, CH * g + k - RAW + 1)
                        load_chunk(g, g - ROWS, k)
                        if store and k == 1:
                            store_row(g - 2)

                def store_row(g):
                    sp.wait_ge(rows_done, g + 1)
                    sp.dma_start(out_v[g - ROWS], done[:, :, :]).then_inc(out_stored, 16)

                for q in range(EARLY * JB):
                    k, j = divmod(q, JB)
                    sp.dma_start(rows[:, q, :], x_v[k, :, j, :]).then_inc(piece_loaded[q], 16)
                    sp.dma_start(half(raw, k, j, WIDE), adj_t[0, k, :, j, :]).then_inc(piece_loaded[q], 16)
                for k in range(EARLY, CH):
                    sp.dma_start(rows[:, k * JB:(k + 1) * JB, :], x_v[k]).then_inc(x_loaded[k - EARLY], 16)
                    if k >= RAW:
                        sp.wait_ge(deg_added, max(k - RAW, 1))
                    load_chunk(0, 0, k)
                    if k == 5:
                        sp.dma_start(w_raw, w_t.rearrange("l p h o -> p l (h o)")).then_inc(w_loaded, 16)
                        sp.dma_start(bias[:, :, :], biases.partition_broadcast(P)).then_inc(bias_loaded, 16)
                with sp.Fori(1, ROWS) as g:
                    load_row_layer0(g)
                for k in range(CH):
                    if k < RAW:
                        sp.wait_ge(deg_added, (CH - 1) * (ROWS - 1) + k - RAW + CH)
                    else:
                        sp.wait_ge(lo_ready, CH * ROWS + k - RAW + 1)
                    load_chunk(ROWS, 0, k)
                load_row_layer1(ROWS + 1, store=False)
                with sp.Fori(ROWS + 2, 2 * ROWS) as g:
                    load_row_layer1(g, store=True)
                store_row(2 * ROWS - 2)
                for b in range(IB):
                    sp.wait_ge(block_done, b + 1)
                    sp.dma_start(out_v[ROWS - 1, :, b, :], done[:, b, :]).then_inc(out_stored, 16)
                sp.wait_ge(out_stored, 16 * (ROWS - 1 + IB))

            @block.scalar
            def _(act):
                def split_chunk(g, k):
                    act.wait_ge(raw_loaded[k % RAW], 16 * (CH // RAW * g + k // RAW + (k % RAW >= EARLY)))
                    if not (isinstance(g, int) and CH * g + k < SPLIT):
                        act.wait_ge(hi_used, CH * g + k - SPLIT + 1)
                        act.wait_ge(lo_ready, CH * g + k - SPLIT + 1)
                    nc.scalar.copy(adj_hi[:, k % SPLIT, :], raw[:, k % RAW, :]).then_inc(hi_ready, 1)

                def split_gathered(g):
                    act.wait_ge(chunk_used, CH * (g + 1))
                    if not same(g, 0):
                        act.wait_ge(lin_ready, IB * g)
                    nc.scalar.copy(gath_hi[:, :], gathered[:, g % 2, :]).then_inc(gath_hi_ready, 1)

                def normalise(g, row, layer):
                    act.wait_ge(shift_ready, g + 1)
                    if layer == 1 and not same(g, ROWS):
                        act.wait_ge(out_stored, 16 * (g - ROWS))
                    for b in range(IB):
                        into = rows[:, row * IB + b, :] if layer == 0 else done[:, b, :]
                        last = nc.scalar.activation(into, summed[:, b, :], ACT.Identity,
                                                    bias=shift[:, b:b + 1], scale=rstd[:, b:b + 1])
                    last.then_inc(rows_done, 1)

                def roots(g, layer):
                    act.wait_ge(row_moments, IB * (g + 1))
                    if layer == 0:
                        nc.scalar.activation(root[:, 1, :], deg[:, :], ACT.Sqrt, bias=eps[:, 1:2])
                    nc.scalar.activation(root[:, 0, :], mean_var[:, :, 1], ACT.Sqrt,
                                         bias=eps[:, 0:1]).then_inc(root_ready, 1)

                def row(g, layer):
                    for k in range(CH):
                        if k == 1:
                            split_gathered(g - 1)
                        if k == 5:
                            roots(g - 1, layer)
                        split_chunk(g, k)
                        if k == 5:
                            normalise(g - 1, g - 1 - layer * ROWS, layer)

                def split_w(layer):
                    nc.scalar.copy(w_hi[:, layer, :], w_raw[:, layer, :]).then_inc(w_hi_ready, 1)

                for q in range(EARLY * JB):
                    k, j = divmod(q, JB)
                    act.wait_ge(piece_loaded[q], 32)
                    feat = nc.scalar.copy(feat_hi[:, q, :], rows[:, q, :])
                    adjacency = nc.scalar.copy(half(adj_hi, k, j, WIDE), half(raw, k, j, WIDE))
                    if j < JB - 1:
                        adjacency.then_inc(piece_hi_ready, 1)
                    else:
                        feat.then_inc(feat_hi_ready, 1)
                        adjacency.then_inc(hi_ready, 1)
                for k in range(EARLY, CH):
                    act.wait_ge(x_loaded[k - EARLY], 16)
                    blocks = slice(k * JB, (k + 1) * JB)
                    nc.scalar.copy(feat_hi[:, blocks, :], rows[:, blocks, :]).then_inc(feat_hi_ready, 1)
                    split_chunk(0, k)
                    if k == 6:
                        act.wait_ge(w_loaded, 16)
                        split_w(0)
                act.wait_ge(constants_ready, 1)
                row(1, 0)
                with act.Fori(2, ROWS) as g:
                    row(g, 0)
                for k in range(CH):
                    if k == 1:
                        split_gathered(ROWS - 1)
                    act.wait_ge(rows_done, k + 1)
                    act.wait_ge(chunk_used, CH * (ROWS - 1) + k + 1)
                    for j in range(k * JB, (k + 1) * JB):
                        last = nc.scalar.activation(feat_hi[:, j, :], rows[:, j, :], ACT.Copy,
                                                    scale=dis[:, j:j + 1])
                    last.then_inc(feat_hi_ready, 1)
                    if k == 5:
                        roots(ROWS - 1, 0)
                    split_chunk(ROWS, k)
                    if k == 2:
                        split_w(1)
                    if k == 5:
                        normalise(ROWS - 1, ROWS - 1, 0)
                row(ROWS + 1, 1)
                with act.Fori(ROWS + 2, 2 * ROWS) as g:
                    row(g, 1)
                g = 2 * ROWS - 1
                act.wait_ge(lin_ready, IB * g)
                for h in range(FH):
                    act.wait_ge(half_summed, h + 1)
                    nc.scalar.copy(gath_hi[:, h * WIDE:(h + 1) * WIDE],
                                   half(gathered, g % 2, h, WIDE)).then_inc(half_hi_ready, 1)
                for b in range(IB + 1):
                    if b < IB:
                        act.wait_ge(row_moments, IB * g + b + 1)
                        nc.scalar.activation(root[:, 0, b:b + 1], mean_var[:, b, 1:2], ACT.Sqrt,
                                             bias=eps[:, 0:1]).then_inc(root_ready, 1)
                    if b == 0:
                        act.wait_ge(out_stored, 16 * (ROWS - 1))
                    else:
                        act.wait_ge(shift_ready, g + b)
                        nc.scalar.activation(done[:, b - 1, :], summed[:, b - 1, :], ACT.Identity,
                                             bias=shift[:, b - 1:b], scale=rstd[:, b - 1:b]
                                             ).then_inc(block_done, 1)

            @block.vector
            def _(dve):
                def split_chunk(g, k):
                    dve.wait_ge(hi_ready, CH * g + k + 1)
                    if not (isinstance(g, int) and CH * g + k < SPLIT):
                        dve.wait_ge(chunk_used, CH * g + k - SPLIT + 1)
                    nc.vector.tensor_tensor(adj_lo[:, k % SPLIT, :], raw[:, k % RAW, :],
                                            adj_hi[:, k % SPLIT, :].bitcast(F32),
                                            ALU.subtract).then_inc(lo_ready, 1)

                def add_degrees(g, k):
                    if k == 1:
                        if not same(g, 0):
                            dve.wait_ge(deg_part_ready, g)
                        nc.vector.tensor_tensor(deg_acc[:, :], raw[:, 0, :], raw[:, 1, :],
                                                ALU.add).then_inc(deg_added, 1)
                    elif k > 1:
                        dve.wait_ge(deg_added, (CH - 1) * g + k - 1)
                        nc.vector.tensor_tensor(deg_acc[:, :], deg_acc[:, :], raw[:, k % RAW, :],
                                                ALU.add).then_inc(deg_added, 1)

                def fold_degrees(g):
                    dve.wait_ge(deg_added, (CH - 1) * (g + 1))
                    nc.vector.tensor_tensor(deg_acc[:, 0:2 * WIDE], deg_acc[:, 0:2 * WIDE],
                                            deg_acc[:, 2 * WIDE:4 * WIDE], ALU.add).then_inc(deg_folded, 1)
                    dve.wait_ge(deg_folded, g + 1)
                    if not same(g, 0):
                        dve.wait_ge(deg_ready, g)
                    nc.vector.tensor_tensor(deg_part[:, :], deg_acc[:, 0:WIDE],
                                            deg_acc[:, WIDE:2 * WIDE], ALU.add).then_inc(deg_part_ready, 1)

                def split_gathered(g):
                    dve.wait_ge(gath_hi_ready, g + 1)
                    nc.vector.tensor_tensor(gath_lo[:, :], gathered[:, g % 2, :], gath_hi[:, :].bitcast(F32),
                                            ALU.subtract).then_inc(gath_lo_ready, 1)

                def sum_rows(g, row, layer, blocks):
                    if blocks[0] == 0 and not same(g, 0):
                        dve.wait_ge(rows_done, g)
                    if blocks[0] == 0 and layer == 0:
                        dve.wait_ge(deg_ready, g + 1)
                    for b in blocks:
                        dve.wait_ge(lin_ready, IB * g + b + 2 - b % 2)
                        if layer == 0:
                            nc.vector.scalar_tensor_tensor(
                                summed[:, b, :], bias[:, 0, :], deg[:, b:b + 1], lin[:, b, :],
                                ALU.mult, ALU.add).then_inc(lin_read, 1)
                        else:
                            nc.vector.scalar_tensor_tensor(
                                summed[:, b, :], lin[:, b, :], dis[:, bass.ds(row * IB + b, 1)],
                                rows[:, row * IB + b, :], ALU.mult, ALU.add).then_inc(lin_read, 1)
                    for b in blocks:
                        dve.wait_ge(lin_read, IB * g + b + 1)
                        other = rows[:, row * IB + b, :] if layer == 0 else bias[:, 1, :]
                        nc.vector.tensor_tensor(summed[:, b, :], summed[:, b, :], other,
                                                ALU.add).then_inc(row_summed, 1)
                    for b in blocks:
                        dve.wait_ge(row_summed, IB * g + b + 1)
                        nc.vector.bn_stats(stats[:, b, :], summed[:, b, :]).then_inc(row_stats, 1)

                def stats_written(g):
                    dve.wait_ge(row_stats, IB * (g + 1))

                def moments(g):
                    for b in range(IB):
                        nc.vector.bn_aggr(mean_var[:, b, :], stats[:, b, :]).then_inc(row_moments, 1)

                def scales(g, row, layer):
                    dve.wait_ge(root_ready, g + 1)
                    if layer == 0:
                        nc.vector.reciprocal(dis[:, bass.ds(row * IB, IB)], root[:, 1, :])
                    nc.vector.reciprocal(rstd[:, :], root[:, 0, :]).then_inc(rstd_ready, 1)
                    dve.wait_ge(rstd_ready, g + 1)
                    nc.vector.scalar_tensor_tensor(shift[:, :], mean_var[:, :, 0], -1.0, rstd[:, :],
                                                   ALU.mult, ALU.mult).then_inc(shift_ready, 1)

                def row(g, layer, features=False):
                    degrees = layer == 0
                    for k in range(CH):
                        if features:
                            split_features(k)
                        if k == 4:
                            stats_written(g - 1)
                        if k == 5:
                            scales(g - 1, g - 1 - layer * ROWS, layer)
                        split_chunk(g, k)
                        if k == 0:
                            if degrees:
                                add_degrees(g - 1, CH - 1)
                            split_gathered(g - 1)
                            if degrees:
                                fold_degrees(g - 1)
                        if k == 2:
                            sum_rows(g - 1, g - 1 - layer * ROWS, layer, range(0, IB // 2))
                        if k == 3:
                            sum_rows(g - 1, g - 1 - layer * ROWS, layer, range(IB // 2, IB))
                        if k == 4:
                            moments(g - 1)
                        if k > 0 and degrees and not features:
                            add_degrees(g, k - 1)

                def split_features(k):
                    dve.wait_ge(feat_hi_ready, CH + k + 1)
                    for j in range(k * JB, (k + 1) * JB):
                        last = nc.vector.scalar_tensor_tensor(
                            feat_lo[:, j, :], rows[:, j, :], dis[:, j:j + 1], feat_hi[:, j, :].bitcast(F32),
                            ALU.mult, ALU.subtract)
                    last.then_inc(feat_lo_ready, 1)

                nc.vector.memset(ones[:, :], 1.0)
                nc.vector.memset(eps[:, 0:1], LN_EPS)
                nc.vector.memset(eps[:, 1:2], DEG_EPS).then_inc(constants_ready, 1)
                for q in range(EARLY * JB):
                    k, j = divmod(q, JB)
                    piece_ready(dve, piece_hi_ready, hi_ready, q)
                    feat = nc.vector.tensor_tensor(feat_lo[:, q, :], rows[:, q, :], feat_hi[:, q, :].bitcast(F32),
                                                   ALU.subtract)
                    adjacency = nc.vector.tensor_tensor(half(adj_lo, k, j, WIDE), half(raw, k, j, WIDE),
                                                        half(adj_hi, k, j, WIDE).bitcast(F32), ALU.subtract)
                    feat.then_inc(piece_feat_lo_ready if j < JB - 1 else feat_lo_ready, 1)
                    adjacency.then_inc(piece_lo_ready if j < JB - 1 else lo_ready, 1)

                def split_w(layer):
                    dve.wait_ge(w_hi_ready, layer + 1)
                    nc.vector.tensor_tensor(w_lo[:, layer, :], w_raw[:, layer, :], w_hi[:, layer, :].bitcast(F32),
                                            ALU.subtract).then_inc(w_lo_ready, 1)

                def split_x(k):
                    blocks = slice(k * JB, (k + 1) * JB)
                    dve.wait_ge(feat_hi_ready, k + 1)
                    nc.vector.tensor_tensor(feat_lo[:, blocks, :], rows[:, blocks, :],
                                            feat_hi[:, blocks, :].bitcast(F32),
                                            ALU.subtract).then_inc(feat_lo_ready, 1)

                add_degrees(0, 1)
                split_x(EARLY)
                for k in range(EARLY, CH):
                    split_chunk(0, k)
                    if k > EARLY:
                        add_degrees(0, k - 1)
                    if k < CH - 1:
                        split_x(k + 1)
                split_w(0)
                dve.wait_ge(bias_loaded, 16)
                row(1, 0)
                with dve.Fori(2, ROWS) as g:
                    row(g, 0)
                row(ROWS, 0, features=True)
                split_w(1)
                row(ROWS + 1, 1)
                with dve.Fori(ROWS + 2, 2 * ROWS) as g:
                    row(g, 1)
                g = 2 * ROWS - 1
                for b in range(IB):
                    last = nc.vector.tensor_tensor(rows[:, N // P - IB + b, :], rows[:, N // P - IB + b, :],
                                                   bias[:, 1, :], ALU.add)
                last.then_inc(residual_ready, 1)
                for h in range(FH):
                    dve.wait_ge(half_hi_ready, h + 1)
                    columns = slice(h * WIDE, (h + 1) * WIDE)
                    nc.vector.tensor_tensor(gath_lo[:, columns], half(gathered, g % 2, h, WIDE),
                                            gath_hi[:, columns].bitcast(F32),
                                            ALU.subtract).then_inc(gath_lo_ready, 1)
                dve.wait_ge(residual_ready, 1)
                dve.wait_ge(rows_done, g)
                for b in range(IB + 2):
                    if b < IB:
                        dve.wait_ge(lin_ready, IB * g + b + 1)
                        nc.vector.scalar_tensor_tensor(
                            summed[:, b, :], last_lin[b], dis[:, N // P - IB + b:N // P - IB + b + 1],
                            rows[:, N // P - IB + b, :], ALU.mult, ALU.add).then_inc(row_summed, 1)
                    if 1 <= b < IB + 1:
                        dve.wait_ge(row_summed, IB * g + b)
                        nc.vector.bn_stats(stats[:, b - 1, :], summed[:, b - 1, :]).then_inc(row_stats, 1)
                    if 2 <= b < IB + 2:
                        dve.wait_ge(root_ready, g + b - 1)
                        nc.vector.reciprocal(rstd[:, b - 2:b - 1], root[:, 0, b - 2:b - 1]).then_inc(rstd_ready, 1)
                    if 1 <= b < IB + 1:
                        dve.wait_ge(row_stats, IB * g + b)
                        nc.vector.bn_aggr(mean_var[:, b - 1, :], stats[:, b - 1, :]).then_inc(row_moments, 1)
                    if 2 <= b < IB + 2:
                        dve.wait_ge(rstd_ready, g + b - 1)
                        nc.vector.scalar_tensor_tensor(shift[:, b - 2:b - 1], mean_var[:, b - 2, 0:1], -1.0,
                                                       rstd[:, b - 2:b - 1], ALU.mult,
                                                       ALU.mult).then_inc(shift_ready, 1)

            @block.tensor
            def _(pe):
                def product(parity, h, k, j, feat, adjacency, start=False, stop=False):
                    return nc.tensor.matmul(half(gathered, parity, h, WIDE), half(feat, k * JB + j, h, P),
                                            half(adjacency, k % SPLIT, j, WIDE), start=start, stop=stop)

                def chunk(g, parity, k):
                    pe.wait_ge(hi_ready, CH * g + k + 1)
                    if isinstance(g, int) and g % ROWS == 0:
                        pe.wait_ge(feat_hi_ready, CH * (g // ROWS) + k + 1)
                        pe.wait_ge(feat_lo_ready, CH * (g // ROWS) + k + 1)
                    for j in range(JB):
                        for h in range(FH):
                            product(parity, h, k, j, feat_lo, adj_hi, start=(k == 0 and j == 0))
                    pe.wait_ge(lo_ready, CH * g + k + 1)
                    for j in range(JB):
                        for h in range(FH):
                            last_hi = product(parity, h, k, j, feat_hi, adj_hi)
                            last = product(parity, h, k, j, feat_hi, adj_lo, stop=(k == CH - 1 and j == JB - 1))
                    last_hi.then_inc(hi_used, 1)
                    last.then_inc(chunk_used, 1)

                def linear_half(b, h, layer, into):
                    columns = slice(h * WIDE + b * P, h * WIDE + (b + 1) * P)
                    for gath, w in ((gath_hi, w_hi), (gath_hi, w_lo), (gath_lo, w_hi)):
                        last = nc.tensor.matmul(into, gath[:, columns], half(w, layer, h, F),
                                                start=(h == 0 and gath is gath_hi and w is w_hi),
                                                stop=(h == FH - 1 and gath is gath_lo))
                    return last

                def linear(g, layer, into):
                    for b in range(IB):
                        for h in range(FH):
                            last = linear_half(b, h, layer, into[b])
                        last.then_inc(lin_ready, 1)

                def degrees(g):
                    if same(g, 0):
                        pe.wait_ge(constants_ready, 1)
                    else:
                        pe.wait_ge(root_ready, g)
                    pe.wait_ge(deg_part_ready, g + 1)
                    for b in range(IB):
                        last = nc.tensor.matmul(deg[:, b:b + 1], deg_part[:, b * P:(b + 1) * P], ones[:, :],
                                                start=True, stop=True)
                    last.then_inc(deg_ready, 1)

                def finish(g, layer):
                    if same(g, 0):
                        pe.wait_ge(w_lo_ready, 1)
                    else:
                        pe.wait_ge(lin_read, IB * g)
                    pe.wait_ge(gath_hi_ready, g + 1)
                    pe.wait_ge(gath_lo_ready, g + 1)
                    linear(g, layer, [lin[:, b, :] for b in range(IB)])

                def row(g, parity, layer):
                    chunk(g, parity, 0)
                    finish(g - 1, layer)
                    if layer == 0:
                        degrees(g - 1)
                    for k in range(1, CH):
                        chunk(g, parity, k)

                for q in range(EARLY * JB):
                    k, j = divmod(q, JB)
                    for feat, adjacency, ready, of_chunk in (
                            (feat_hi, adj_hi, piece_hi_ready, hi_ready),
                            (feat_lo, adj_hi, piece_feat_lo_ready, feat_lo_ready),
                            (feat_hi, adj_lo, piece_lo_ready, lo_ready)):
                        piece_ready(pe, ready, of_chunk, q)
                        for h in range(FH):
                            last = product(0, h, k, j, feat, adjacency, start=(q == 0 and ready is piece_hi_ready))
                        if j == JB - 1 and ready is piece_feat_lo_ready:
                            last.then_inc(hi_used, 1)
                    if j == JB - 1:
                        last.then_inc(chunk_used, 1)
                for k in range(EARLY, CH):
                    chunk(0, 0, k)
                row(1, 1, 0)
                with pe.Fori(2, ROWS, 2) as g:
                    row(g, 0, 0)
                    row(g + 1, 1, 0)
                row(ROWS, 0, 0)
                pe.wait_ge(w_lo_ready, 2)
                with pe.Fori(ROWS + 1, 2 * ROWS - 1, 2) as g:
                    row(g, 1, 1)
                    row(g + 1, 0, 1)
                g = 2 * ROWS - 1
                chunk(g, 1, 0)
                finish(g - 1, 1)
                for k in range(1, CH - 1):
                    chunk(g, 1, k)
                pe.wait_ge(hi_ready, CH * (g + 1))
                pe.wait_ge(lo_ready, CH * (g + 1))
                for h in range(FH):
                    for j in range(JB):
                        product(1, h, CH - 1, j, feat_lo, adj_hi)
                        product(1, h, CH - 1, j, feat_hi, adj_hi)
                        last = product(1, h, CH - 1, j, feat_hi, adj_lo, stop=(j == JB - 1))
                    last.then_inc(half_summed, 1)
                pe.wait_ge(lin_read, IB * g)
                for h in range(FH):
                    pe.wait_ge(half_hi_ready, h + 1)
                    pe.wait_ge(gath_lo_ready, g + h + 1)
                    for b in range(IB):
                        last = linear_half(b, h, 1, last_lin[b])
                        if h == FH - 1:
                            last.then_inc(lin_ready, 1)


def kernel(x, adj, L0_gnn_W, L0_gnn_b, L1_gnn_W, L1_gnn_b):
    import numpy as np
    import concourse.bacc as bacc
    from concourse.bass_utils import run_bass_kernel_spmd

    adj_t = np.ascontiguousarray(
        np.asarray(adj).reshape(ROWS, WIDE, CH, JB, P).transpose(0, 2, 4, 3, 1))
    w_t = np.ascontiguousarray(np.stack(
        [np.asarray(w).T.reshape(FH, P, F).transpose(1, 0, 2) for w in (L0_gnn_W, L1_gnn_W)]))
    arrays = {
        "x": np.ascontiguousarray(x), "adj_t": adj_t, "w_t": w_t,
        "biases": np.stack([np.asarray(L0_gnn_b), np.asarray(L1_gnn_b)]),
    }
    nc = bacc.Bacc("TRN2", target_bir_lowering=False, num_devices=1)
    args = [nc.dram_tensor(n, a.shape, mybir.dt.from_np(a.dtype), kind="ExternalInput").ap()
            for n, a in arrays.items()]
    out = nc.dram_tensor("out", (N, F), F32, kind="ExternalOutput").ap()
    graph_layers(nc, *args, out)
    got = run_bass_kernel_spmd(nc, [arrays], core_ids=[0])
    return got.results[0]["out"]
```
